# Optimizing a Trainium2 kernel written in Bass

```python
import numpy as np
import jax
import jax.numpy as jnp

def _softmax(x, axis=-1):
    return jax.nn.softmax(x, axis=axis)

def _gelu(x):
    return jax.nn.gelu(x, approximate=True)

def _silu(x):
    return jax.nn.silu(x)

def _sigmoid(x):
    return jax.nn.sigmoid(x)

def _layernorm(x, axis=-1, eps=1e-05):
    m = jnp.mean(x, axis=axis, keepdims=True)
    v = jnp.var(x, axis=axis, keepdims=True)
    return (x - m) / jnp.sqrt(v + eps)

def _scatter_add(tgt, idx, src, axis=0):
    return tgt.at[idx].add(src)

def _segment_sum(src, seg, n):
    return jax.ops.segment_sum(src, seg, n)
kernel_name = 'mk_dlrm_tower_d1_rec_r8_5de726'

def setup_inputs(seed: int=0):
    np.random.seed(seed)
    _w = jnp.asarray

    def _rec_inputs():
        import jax
        import jax.numpy as jnp
        _tk = jax.random.key(seed)
        dense_ctx = jax.random.normal(jax.random.fold_in(_tk, 190), (1024, 16), jnp.float32)
        ids = jnp.stack([jax.random.randint(jax.random.fold_in(_tk, 200 + f), (1024,), 0, v, jnp.int32) for f, v in enumerate([125000, 125000, 12500, 1250, 1000, 1000, 12500, 1000, 1250, 1250, 125000, 12500, 1250, 1000, 12500, 1250, 1250, 1250, 1000, 1250, 1250, 1250, 1250, 1000, 1000, 1000, 1250, 12500, 12500, 1250, 12500, 1250])], axis=1)
        tbl_0 = 0.05 * jax.random.normal(jax.random.fold_in(_tk, 500 + 0), (125000, 64), jnp.float32)
        tbl_1 = 0.05 * jax.random.normal(jax.random.fold_in(_tk, 500 + 1), (125000, 64), jnp.float32)
        tbl_2 = 0.05 * jax.random.normal(jax.random.fold_in(_tk, 500 + 2), (12500, 64), jnp.float32)
        tbl_3 = 0.05 * jax.random.normal(jax.random.fold_in(_tk, 500 + 3), (1250, 64), jnp.float32)
        tbl_4 = 0.05 * jax.random.normal(jax.random.fold_in(_tk, 500 + 4), (1000, 64), jnp.float32)
        tbl_5 = 0.05 * jax.random.normal(jax.random.fold_in(_tk, 500 + 5), (1000, 64), jnp.float32)
        tbl_6 = 0.05 * jax.random.normal(jax.random.fold_in(_tk, 500 + 6), (12500, 64), jnp.float32)
        tbl_7 = 0.05 * jax.random.normal(jax.random.fold_in(_tk, 500 + 7), (1000, 64), jnp.float32)
        tbl_8 = 0.05 * jax.random.normal(jax.random.fold_in(_tk, 500 + 8), (1250, 64), jnp.float32)
        tbl_9 = 0.05 * jax.random.normal(jax.random.fold_in(_tk, 500 + 9), (1250, 64), jnp.float32)
        tbl_10 = 0.05 * jax.random.normal(jax.random.fold_in(_tk, 500 + 10), (125000, 64), jnp.float32)
        tbl_11 = 0.05 * jax.random.normal(jax.random.fold_in(_tk, 500 + 11), (12500, 64), jnp.float32)
        tbl_12 = 0.05 * jax.random.normal(jax.random.fold_in(_tk, 500 + 12), (1250, 64), jnp.float32)
        tbl_13 = 0.05 * jax.random.normal(jax.random.fold_in(_tk, 500 + 13), (1000, 64), jnp.float32)
        tbl_14 = 0.05 * jax.random.normal(jax.random.fold_in(_tk, 500 + 14), (12500, 64), jnp.float32)
        tbl_15 = 0.05 * jax.random.normal(jax.random.fold_in(_tk, 500 + 15), (1250, 64), jnp.float32)
        tbl_16 = 0.05 * jax.random.normal(jax.random.fold_in(_tk, 500 + 16), (1250, 64), jnp.float32)
        tbl_17 = 0.05 * jax.random.normal(jax.random.fold_in(_tk, 500 + 17), (1250, 64), jnp.float32)
        tbl_18 = 0.05 * jax.random.normal(jax.random.fold_in(_tk, 500 + 18), (1000, 64), jnp.float32)
        tbl_19 = 0.05 * jax.random.normal(jax.random.fold_in(_tk, 500 + 19), (1250, 64), jnp.float32)
        tbl_20 = 0.05 * jax.random.normal(jax.random.fold_in(_tk, 500 + 20), (1250, 64), jnp.float32)
        tbl_21 = 0.05 * jax.random.normal(jax.random.fold_in(_tk, 500 + 21), (1250, 64), jnp.float32)
        tbl_22 = 0.05 * jax.random.normal(jax.random.fold_in(_tk, 500 + 22), (1250, 64), jnp.float32)
        tbl_23 = 0.05 * jax.random.normal(jax.random.fold_in(_tk, 500 + 23), (1000, 64), jnp.float32)
        tbl_24 = 0.05 * jax.random.normal(jax.random.fold_in(_tk, 500 + 24), (1000, 64), jnp.float32)
        tbl_25 = 0.05 * jax.random.normal(jax.random.fold_in(_tk, 500 + 25), (1000, 64), jnp.float32)
        tbl_26 = 0.05 * jax.random.normal(jax.random.fold_in(_tk, 500 + 26), (1250, 64), jnp.float32)
        tbl_27 = 0.05 * jax.random.normal(jax.random.fold_in(_tk, 500 + 27), (12500, 64), jnp.float32)
        tbl_28 = 0.05 * jax.random.normal(jax.random.fold_in(_tk, 500 + 28), (12500, 64), jnp.float32)
        tbl_29 = 0.05 * jax.random.normal(jax.random.fold_in(_tk, 500 + 29), (1250, 64), jnp.float32)
        tbl_30 = 0.05 * jax.random.normal(jax.random.fold_in(_tk, 500 + 30), (12500, 64), jnp.float32)
        tbl_31 = 0.05 * jax.random.normal(jax.random.fold_in(_tk, 500 + 31), (1250, 64), jnp.float32)
        _rk = jax.random.fold_in(_tk, 7)
        W_top1 = 0.0441942 * jax.random.normal(jax.random.fold_in(_tk, 801), (512, 512), jnp.float32)
        W_top2 = 0.0441942 * jax.random.normal(jax.random.fold_in(_tk, 802), (512, 256), jnp.float32)
        W_top3 = 0.0625 * jax.random.normal(jax.random.fold_in(_tk, 803), (256, 1), jnp.float32)
        b_top1 = jnp.zeros((512,), jnp.float32)
        b_top2 = jnp.zeros((256,), jnp.float32)
        return (dense_ctx, ids, tbl_0, tbl_1, tbl_2, tbl_3, tbl_4, tbl_5, tbl_6, tbl_7, tbl_8, tbl_9, tbl_10, tbl_11, tbl_12, tbl_13, tbl_14, tbl_15, tbl_16, tbl_17, tbl_18, tbl_19, tbl_20, tbl_21, tbl_22, tbl_23, tbl_24, tbl_25, tbl_26, tbl_27, tbl_28, tbl_29, tbl_30, tbl_31, W_top1, b_top1, W_top2, b_top2, W_top3)
    dense_ctx, ids, tbl_0, tbl_1, tbl_2, tbl_3, tbl_4, tbl_5, tbl_6, tbl_7, tbl_8, tbl_9, tbl_10, tbl_11, tbl_12, tbl_13, tbl_14, tbl_15, tbl_16, tbl_17, tbl_18, tbl_19, tbl_20, tbl_21, tbl_22, tbl_23, tbl_24, tbl_25, tbl_26, tbl_27, tbl_28, tbl_29, tbl_30, tbl_31, W_top1, b_top1, W_top2, b_top2, W_top3 = _rec_inputs()

    def _L0_rec_setup():
        import jax, jax.numpy as jnp
        import numpy as np
        B = 256
        NUM_FIELDS = 32
        EMBED = 64
        P = NUM_FIELDS * (NUM_FIELDS - 1) // 2
        _ROW, _COL = np.triu_indices(NUM_FIELDS, k=1)
        ROW_IDX = jnp.asarray(_ROW, dtype=jnp.int32)
        COL_IDX = jnp.asarray(_COL, dtype=jnp.int32)
        key = jax.random.key(seed)
        k1, k2 = jax.random.split(key)
        emb_inputs = jax.random.normal(k1, (B, NUM_FIELDS, EMBED), dtype=jnp.float32)
        fan_in = P * EMBED
        fan_out = EMBED
        std = float(np.sqrt(2.0 / (fan_in + fan_out)))
        kernel = jax.random.normal(k2, (EMBED, P, EMBED), dtype=jnp.float32) * std
        return {'emb_inputs': emb_inputs, 'kernel': kernel}
    _L0_rec_all = _L0_rec_setup()
    _L0_rec_in = {k: v for k, v in _L0_rec_all.items() if k in ('kernel',)}
    del _L0_rec_all
    return {'dense_ctx': dense_ctx, 'ids': ids, 'tbl_0': tbl_0, 'tbl_1': tbl_1, 'tbl_2': tbl_2, 'tbl_3': tbl_3, 'tbl_4': tbl_4, 'tbl_5': tbl_5, 'tbl_6': tbl_6, 'tbl_7': tbl_7, 'tbl_8': tbl_8, 'tbl_9': tbl_9, 'tbl_10': tbl_10, 'tbl_11': tbl_11, 'tbl_12': tbl_12, 'tbl_13': tbl_13, 'tbl_14': tbl_14, 'tbl_15': tbl_15, 'tbl_16': tbl_16, 'tbl_17': tbl_17, 'tbl_18': tbl_18, 'tbl_19': tbl_19, 'tbl_20': tbl_20, 'tbl_21': tbl_21, 'tbl_22': tbl_22, 'tbl_23': tbl_23, 'tbl_24': tbl_24, 'tbl_25': tbl_25, 'tbl_26': tbl_26, 'tbl_27': tbl_27, 'tbl_28': tbl_28, 'tbl_29': tbl_29, 'tbl_30': tbl_30, 'tbl_31': tbl_31, 'W_top1': W_top1, 'b_top1': b_top1, 'W_top2': W_top2, 'b_top2': b_top2, 'W_top3': W_top3, 'L0_rec_kernel': _L0_rec_in['kernel']}

def reference(dense_ctx, ids, tbl_0, tbl_1, tbl_2, tbl_3, tbl_4, tbl_5, tbl_6, tbl_7, tbl_8, tbl_9, tbl_10, tbl_11, tbl_12, tbl_13, tbl_14, tbl_15, tbl_16, tbl_17, tbl_18, tbl_19, tbl_20, tbl_21, tbl_22, tbl_23, tbl_24, tbl_25, tbl_26, tbl_27, tbl_28, tbl_29, tbl_30, tbl_31, W_top1, b_top1, W_top2, b_top2, W_top3, L0_rec_kernel):
    import jax
    import jax.numpy as jnp

    def _L0_rec_ref(emb_inputs, kernel):
        import jax, jax.numpy as jnp
        import numpy as np
        B = 256
        NUM_FIELDS = 32
        EMBED = 64
        P = NUM_FIELDS * (NUM_FIELDS - 1) // 2
        _ROW, _COL = np.triu_indices(NUM_FIELDS, k=1)
        ROW_IDX = jnp.asarray(_ROW, dtype=jnp.int32)
        COL_IDX = jnp.asarray(_COL, dtype=jnp.int32)
        p = emb_inputs[:, ROW_IDX]
        q = emb_inputs[:, COL_IDX]
        return jnp.einsum('bne,hne,bnh->bn', p, kernel, q)
    e = jnp.stack([tbl_0[ids[:, 0]], tbl_1[ids[:, 1]], tbl_2[ids[:, 2]], tbl_3[ids[:, 3]], tbl_4[ids[:, 4]], tbl_5[ids[:, 5]], tbl_6[ids[:, 6]], tbl_7[ids[:, 7]], tbl_8[ids[:, 8]], tbl_9[ids[:, 9]], tbl_10[ids[:, 10]], tbl_11[ids[:, 11]], tbl_12[ids[:, 12]], tbl_13[ids[:, 13]], tbl_14[ids[:, 14]], tbl_15[ids[:, 15]], tbl_16[ids[:, 16]], tbl_17[ids[:, 17]], tbl_18[ids[:, 18]], tbl_19[ids[:, 19]], tbl_20[ids[:, 20]], tbl_21[ids[:, 21]], tbl_22[ids[:, 22]], tbl_23[ids[:, 23]], tbl_24[ids[:, 24]], tbl_25[ids[:, 25]], tbl_26[ids[:, 26]], tbl_27[ids[:, 27]], tbl_28[ids[:, 28]], tbl_29[ids[:, 29]], tbl_30[ids[:, 30]], tbl_31[ids[:, 31]]], axis=1)
    z = _L0_rec_ref(e, L0_rec_kernel)
    z = z.reshape(z.shape[0], -1)
    h = jnp.concatenate([z, dense_ctx], axis=1)
    h = jnp.maximum(h @ W_top1 + b_top1, 0.0)
    h = jnp.maximum(h @ W_top2 + b_top2, 0.0)
    y = h @ W_top3
    return y

_drawn_inputs = setup_inputs


def setup_inputs(seed=0):
    import zlib

    import numpy as np

    out = dict(_drawn_inputs(seed))
    spreads = {'b_top1': (0.0, 0.1), 'b_top2': (0.0, 0.1)}
    factors = {'tbl_0': 8.0,
     'tbl_1': 8.0,
     'tbl_2': 8.0,
     'tbl_3': 8.0,
     'tbl_4': 8.0,
     'tbl_5': 8.0,
     'tbl_6': 8.0,
     'tbl_7': 8.0,
     'tbl_8': 8.0,
     'tbl_9': 8.0,
     'tbl_10': 8.0,
     'tbl_11': 8.0,
     'tbl_12': 8.0,
     'tbl_13': 8.0,
     'tbl_14': 8.0,
     'tbl_15': 8.0,
     'tbl_16': 8.0,
     'tbl_17': 8.0,
     'tbl_18': 8.0,
     'tbl_19': 8.0,
     'tbl_20': 8.0,
     'tbl_21': 8.0,
     'tbl_22': 8.0,
     'tbl_23': 8.0,
     'tbl_24': 8.0,
     'tbl_25': 8.0,
     'tbl_26': 8.0,
     'tbl_27': 8.0,
     'tbl_28': 8.0,
     'tbl_29': 8.0,
     'tbl_30': 8.0,
     'tbl_31': 8.0,
     'L0_rec_kernel': 8.0}
    for name, (base, spread) in spreads.items():
        noise = np.random.default_rng([zlib.crc32(name.encode()), seed]).standard_normal(out[name].shape)
        drawn = base * np.exp(spread * noise) if base else spread * noise
        out[name] = jnp.asarray(drawn.astype(out[name].dtype))
    for name, factor in factors.items():
        out[name] = (out[name] * factor).astype(out[name].dtype)
    return out
```

```python
from contextlib import ExitStack

import numpy as np

import concourse.bass as bass
from concourse import mybir

F32 = mybir.dt.float32
F32R = mybir.dt.float32r
I32 = mybir.dt.int32
ALU = mybir.AluOpType
ACT = mybir.ActivationFunctionType

P = 128
BATCH, FIELDS, EMBED, DENSE = 1024, 32, 64, 16
HIDDEN1, HIDDEN2 = 512, 256
HALVES = 2
HB = BATCH // HALVES
SUBS = HB // P
TILES = BATCH // P
COUPLES = FIELDS // 2

BLOCKS = [(j, m) for j in range(1, FIELDS) for m in range((j + 1) // 2)]
NBLK = len(BLOCKS)
QUAD = 4
QUADS = NBLK // QUAD
DUOS = NBLK // 2
GROUP_QUADS = P // (2 * QUAD)
GROUPS = QUADS // GROUP_QUADS
CHUNK_QUADS = 4
CHUNKS = QUADS // CHUNK_QUADS
MT1, MT2 = HIDDEN1 // P, HIDDEN2 // P

K_RING, S_RING, E_RING, G_RING, Y_RING = 3, 4, 3, 3, 4


def pair_index(i, j):
    return i * (2 * FIELDS - i - 1) // 2 + j - i - 1


def z_row(q, s):
    g, r = divmod(q, GROUP_QUADS * QUAD)
    return g, 32 * (r % QUAD) + 2 * (r // QUAD) + s


LONE = [q for q, (j, m) in enumerate(BLOCKS) if 2 * m + 1 == j]
FIRST_BLOCK = [next(q for q, (j, _) in enumerate(BLOCKS) if j // 2 == m) for m in range(COUPLES)]
END_BLOCK = FIRST_BLOCK[1:] + [NBLK]


def couple_quad(h, m):
    need = h * QUADS + FIRST_BLOCK[m] // QUAD
    ahead = 0 if h == 0 and m < 6 else 2
    return max(need - ahead, 0)


COUPLES_AT = [[] for _ in range(HALVES * QUADS)]
for _h in range(HALVES):
    for _m in range(COUPLES):
        COUPLES_AT[couple_quad(_h, _m)].append((_h, _m))

HEAD_AT = {QUADS + 3 + n: ("l1", n) for n in range(MT1)}
HEAD_AT |= {QUADS + 3 + MT1 + 2 + n: ("l2", n) for n in range(MT2)}
HEAD_AT[QUADS + 3 + MT1 + 2 + MT2 + 2] = ("l3", 0)
HEAD_STEPS = MT1 + MT2 + 1


def interaction_tower(nc, ids, tables, dense_rows, k_blocks, w1, b1, w2, b2, w3, ident, selector, y):
    ctx = ExitStack()
    with ctx:
        def sb(name, shape, dt=F32):
            return ctx.enter_context(nc.sbuf_tensor(name, shape, dt))

        def pb(name, shape):
            return ctx.enter_context(nc.psum_tensor(name, shape, F32))

        def sem(name):
            return ctx.enter_context(nc.semaphore(name))

        ids_sb = sb("ids_sb", [P, TILES, FIELDS], I32)
        ident_sb = sb("ident_sb", [P, P])
        sel_sb = sb("sel_sb", [P, GROUP_QUADS, 32])
        b1_sb = sb("b1_sb", [P, MT1])
        b2_sb = sb("b2_sb", [P, MT2])
        w1_sb = sb("w1_sb", [P, GROUPS, HIDDEN1])
        w2_sb = sb("w2_sb", [P, MT1, HIDDEN2])
        w3_sb = sb("w3_sb", [P, MT2])
        gathered = sb("gathered", [P, G_RING, SUBS, P])
        k_raw = sb("k_raw", [P, K_RING, CHUNK_QUADS, QUAD * P])
        k_hi = sb("k_hi", [P, S_RING, QUAD * P], F32R)
        k_lo = sb("k_lo", [P, S_RING, QUAD * P], F32R)
        emb = sb("emb", [P, HALVES, COUPLES, HB])
        split = sb("split", [P, E_RING, 2, HB], F32R)
        prod = sb("prod", [P, Y_RING, 2 * HB])
        z_sb = sb("z_sb", [P, GROUPS, HB])
        h1_sb = sb("h1_sb", [P, MT1, HB])
        h2_sb = sb("h2_sb", [P, MT2, HB])
        y_sb = sb("y_sb", [P, TILES])

        bil = [pb(f"bil{i}", [P, 2 * HB]) for i in range(2)]
        z_ps = [pb(f"z_ps{i}", [P, HB]) for i in range(2)]
        couple_ps = pb("couple_ps", [P, HB])
        head_ps = pb("head_ps", [P, HB])

        ids_loaded = sem("ids_loaded")
        consts_loaded = sem("consts_loaded")
        head_loaded = sem("head_loaded")
        couple_gathered = [sem(f"couple_gathered{i}") for i in range(G_RING)]
        k_loaded = [sem(f"k_loaded{i}") for i in range(K_RING)]
        couple_transposed = sem("couple_transposed")
        emb_kept = sem("emb_kept")
        emb_lo = sem("emb_lo")
        k_hi_ready = sem("k_hi_ready")
        k_lo_ready = sem("k_lo_ready")
        block_done = sem("block_done")
        duo_multiplied = sem("duo_multiplied")
        quad_reduced = sem("quad_reduced")
        z_copied = sem("z_copied")
        dense_placed = [sem(f"dense_placed{g}") for g in range(GROUPS)]
        head_done = sem("head_done")
        head_kept = sem("head_kept")
        y_stored = sem("y_stored")

        def rows_placed(h, g):
            return 16 * (h + 1) * sum(z_row(q, 1)[0] == g for q in LONE)

        block = ctx.enter_context(nc.Block())

        @block.sync
        def _(sp):
            sp.dma_start(ids_sb[:, :, :], ids.rearrange("(p t) f -> p t f", p=P)).then_inc(ids_loaded, 16)

            def load_chunk(n):
                if n >= K_RING:
                    sp.wait_ge(k_hi_ready, (n - K_RING + 1) * CHUNK_QUADS)
                    sp.wait_ge(k_lo_ready, (n - K_RING + 1) * CHUNK_QUADS)
                c = n % CHUNKS
                src = k_blocks[:, c * CHUNK_QUADS * QUAD * P:(c + 1) * CHUNK_QUADS * QUAD * P]
                for d in range(2):
                    dst = k_raw[d * EMBED:(d + 1) * EMBED, n % K_RING, :, :].rearrange("p q n -> p (q n)")
                    sp.dma_start(dst, src).then_inc(k_loaded[n % K_RING], 16)

            def place_dense(group):
                h, g = divmod(group, GROUPS)
                sp.wait_ge(z_copied, group + 1)
                for f, q in enumerate(LONE):
                    zg, row = z_row(q, 1)
                    if zg == g:
                        sp.dma_start(z_sb[row:row + 1, g, :], dense_rows[f:f + 1, h * HB:(h + 1) * HB])\
                          .then_inc(dense_placed[g], 16)

            load_chunk(0)
            sp.dma_start(ident_sb[:, :], ident).then_inc(consts_loaded, 16)
            sp.dma_start(sel_sb[:, :, :], selector.rearrange("p (k c) -> p k c", c=32)).then_inc(consts_loaded, 16)
            load_chunk(1)
            load_chunk(2)
            sp.dma_start(w1_sb[:, :, :], w1.rearrange("(g p) n -> p g n", p=P)).then_inc(head_loaded, 16)
            sp.dma_start(w2_sb[:, :, :], w2.rearrange("(g p) n -> p g n", p=P)).then_inc(head_loaded, 16)
            sp.dma_start(w3_sb[:, :], w3).then_inc(head_loaded, 16)
            sp.dma_start(b1_sb[:, :], b1).then_inc(head_loaded, 16)
            sp.dma_start(b2_sb[:, :], b2).then_inc(head_loaded, 16)
            for n in range(K_RING, HALVES * CHUNKS):
                group, left = divmod(n - 3, GROUP_QUADS // CHUNK_QUADS)
                if left == 0 and group >= 1:
                    place_dense(group - 1)
                load_chunk(n)
            place_dense(HALVES * GROUPS - 1)
            sp.wait_ge(head_kept, HALVES * HEAD_STEPS)
            sp.dma_start(y.rearrange("(p t) o -> p (t o)", p=P), y_sb[:, :]).then_inc(y_stored, 16)
            sp.wait_ge(y_stored, 16)

        @block.gpsimd
        def _(pool):
            pool.wait_ge(ids_loaded, 16)
            for h in range(HALVES):
                for m in range(COUPLES):
                    n = h * COUPLES + m
                    if n >= G_RING:
                        pool.wait_ge(couple_transposed, n - G_RING + 1)
                    for s in range(2):
                        for t in range(SUBS):
                            f = 2 * m + s
                            pool.indirect_dma_start(
                                gathered[:, n % G_RING, t, s * EMBED:(s + 1) * EMBED], None, tables[f],
                                bass.IndirectOffsetOnAxis(ap=ids_sb[:, h * SUBS + t, f:f + 1], axis=0),
                            ).then_inc(couple_gathered[n % G_RING], 16)

        @block.scalar
        def _(act):
            def split_hi(q):
                chunk = q // CHUNK_QUADS
                act.wait_ge(k_loaded[chunk % K_RING], 32 * (chunk // K_RING + 1))
                if q >= S_RING:
                    act.wait_ge(block_done, QUAD * (q - S_RING + 1))
                act.activation(k_hi[:, q % S_RING, :], k_raw[:, chunk % K_RING, q % CHUNK_QUADS, :], ACT.Copy)\
                   .then_inc(k_hi_ready, 1)

            def keep_couple(h, m):
                n = h * COUPLES + m
                act.wait_ge(couple_transposed, n + 1)
                if n >= E_RING:
                    ph, pm = divmod(n - E_RING, COUPLES)
                    act.wait_ge(block_done, ph * NBLK + END_BLOCK[pm])
                act.activation(emb[:, h, m, :], couple_ps[:, :], ACT.Copy)
                if m > 0:
                    act.activation(split[0:EMBED, n % E_RING, 0, :], couple_ps[0:EMBED, :], ACT.Copy)
                act.activation(split[EMBED:P, n % E_RING, 1, :], couple_ps[EMBED:P, :], ACT.Copy).then_inc(emb_kept, 1)

            def copy_z(group):
                act.wait_ge(quad_reduced, (group + 1) * GROUP_QUADS)
                if group >= GROUPS:
                    act.wait_ge(head_done, (group // GROUPS - 1) * HEAD_STEPS + MT1)
                act.activation(z_sb[:, group % GROUPS, :], z_ps[group % 2][:, :], ACT.Copy).then_inc(z_copied, 1)

            def keep_head(h, kind, n, bank):
                step = {"l1": n, "l2": MT1 + n, "l3": MT1 + MT2}[kind]
                act.wait_ge(head_done, h * HEAD_STEPS + step + 1)
                if kind == "l1":
                    act.activation(h1_sb[:, n, :], bank, ACT.Relu, bias=b1_sb[:, n:n + 1]).then_inc(head_kept, 1)
                elif kind == "l2":
                    act.activation(h2_sb[:, n, :], bank, ACT.Relu, bias=b2_sb[:, n:n + 1]).then_inc(head_kept, 1)
                else:
                    act.activation(y_sb[:, h * SUBS:(h + 1) * SUBS], bank[:, 0:SUBS], ACT.Copy).then_inc(head_kept, 1)

            act.wait_ge(head_loaded, 16 * 5)
            split_hi(0)
            split_hi(1)
            for q in range(HALVES * QUADS):
                for h, m in COUPLES_AT[q]:
                    keep_couple(h, m)
                if q + 2 < HALVES * QUADS:
                    split_hi(q + 2)
                if q and q % GROUP_QUADS == 0:
                    copy_z(q // GROUP_QUADS - 1)
                if q in HEAD_AT:
                    keep_head(0, *HEAD_AT[q], head_ps[:, :])
            copy_z(HALVES * GROUPS - 1)
            for n in range(MT1):
                keep_head(HALVES - 1, "l1", n, bil[n // 2][:, n % 2 * HB:(n % 2 + 1) * HB])
            for n in range(MT2):
                keep_head(HALVES - 1, "l2", n, z_ps[n][:, :])
            keep_head(HALVES - 1, "l3", 0, head_ps[:, :])

        @block.vector
        def _(dve):
            def split_lo(q):
                chunk = q // CHUNK_QUADS
                dve.wait_ge(k_hi_ready, q + 1)
                dve.tensor_tensor(k_lo[:, q % S_RING, :], k_raw[:, chunk % K_RING, q % CHUNK_QUADS, :],
                                  k_hi[:, q % S_RING, :].bitcast(F32), ALU.subtract).then_inc(k_lo_ready, 1)

            def split_couple(h, m):
                n = h * COUPLES + m
                dve.wait_ge(emb_kept, n + 1)
                if m > 0:
                    dve.tensor_tensor(split[EMBED:P, n % E_RING, 0, :], emb[0:EMBED, h, m, :],
                                      split[0:EMBED, n % E_RING, 0, :].bitcast(F32), ALU.subtract)
                dve.tensor_tensor(split[0:EMBED, n % E_RING, 1, :], emb[EMBED:P, h, m, :],
                                  split[EMBED:P, n % E_RING, 1, :].bitcast(F32), ALU.subtract).then_inc(emb_lo, 1)

            def multiply(d):
                h, first = divmod(2 * d, NBLK)
                ma, mb = BLOCKS[first][1], BLOCKS[first + 1][1]
                dve.wait_ge(block_done, 2 * d + 2)
                if d >= Y_RING:
                    dve.wait_ge(quad_reduced, (d - Y_RING) // 2 + 1)
                dve.wait_ge(emb_kept, h * COUPLES + max(BLOCKS[first][0], BLOCKS[first + 1][0]) // 2 + 1)
                out = prod[:, d % Y_RING, :]
                if mb > ma:
                    dve.tensor_tensor(out.rearrange("p (b n) -> p b n", b=2),
                                      bil[d % 2][:, :].rearrange("p (b n) -> p b n", b=2),
                                      emb[:, h, ma:mb + 1:mb - ma, :], ALU.mult).then_inc(duo_multiplied, 1)
                else:
                    dve.tensor_tensor(out[:, 0:HB], bil[d % 2][:, 0:HB], emb[:, h, ma, :], ALU.mult)
                    dve.tensor_tensor(out[:, HB:2 * HB], bil[d % 2][:, HB:2 * HB], emb[:, h, mb, :], ALU.mult)\
                       .then_inc(duo_multiplied, 1)

            split_lo(0)
            for q in range(HALVES * QUADS):
                for h, m in COUPLES_AT[q]:
                    split_couple(h, m)
                multiply(2 * q)
                if q + 1 < HALVES * QUADS:
                    split_lo(q + 1)
                multiply(2 * q + 1)

        @block.tensor
        def _(pe):
            def transpose_couple(h, m):
                n = h * COUPLES + m
                pe.wait_ge(couple_gathered[n % G_RING], 16 * 2 * SUBS * (n // G_RING + 1))
                if n:
                    pe.wait_ge(emb_kept, n)
                for t in range(SUBS):
                    last = pe.transpose(couple_ps[:, t * P:(t + 1) * P], gathered[:, n % G_RING, t, :], ident_sb[:, :])
                last.then_inc(couple_transposed, 1)

            def bilinear(b):
                h, q = divmod(b, NBLK)
                j, _ = BLOCKS[q]
                n = h * COUPLES + j // 2
                quad, at = divmod(b, QUAD)
                if at == 0:
                    pe.wait_ge(k_lo_ready, quad + 1)
                if q == 0 or BLOCKS[q - 1][0] // 2 != j // 2:
                    pe.wait_ge(emb_lo, n + 1)
                if b % 2 == 0 and b >= 4:
                    pe.wait_ge(duo_multiplied, b // 2 - 1)
                out = bil[b // 2 % 2][:, b % 2 * HB:(b % 2 + 1) * HB]
                moving = split[:, n % E_RING, j % 2, :]
                cols = slice(at * P, (at + 1) * P)
                pe.matmul(out, k_hi[:, quad % S_RING, cols], moving, start=True, stop=False)
                pe.matmul(out, k_lo[:, quad % S_RING, cols], moving, start=False, stop=True).then_inc(block_done, 1)

            def reduce_quad(q):
                group, k = divmod(q, GROUP_QUADS)
                pe.wait_ge(duo_multiplied, 2 * q + 2)
                if k == 0 and group >= 2:
                    pe.wait_ge(z_copied, group - 1)
                for c in range(QUAD):
                    d = 2 * q + c // 2
                    last = pe.matmul(z_ps[group % 2][32 * c:32 * (c + 1), :], sel_sb[:, k, :],
                                     prod[:, d % Y_RING, c % 2 * HB:(c % 2 + 1) * HB],
                                     start=k == 0, stop=k == GROUP_QUADS - 1, tile_position=(0, 32 * c))
                last.then_inc(quad_reduced, 1)

            def head(h, kind, n, bank):
                before = h * HEAD_STEPS
                if kind == "l1":
                    if h == 0:
                        pe.wait_ge(head_kept, before + n)
                    for g in range(GROUPS):
                        pe.wait_ge(z_copied, h * GROUPS + g + 1)
                        pe.wait_ge(dense_placed[g], rows_placed(h, g))
                        last = pe.matmul(bank, w1_sb[:, g, n * P:(n + 1) * P], z_sb[:, g, :],
                                         start=g == 0, stop=g == GROUPS - 1)
                elif kind == "l2":
                    pe.wait_ge(head_kept, before + MT1 + (n if h == 0 else 0))
                    for g in range(MT1):
                        last = pe.matmul(bank, w2_sb[:, g, n * P:(n + 1) * P], h1_sb[:, g, :],
                                         start=g == 0, stop=g == MT1 - 1)
                else:
                    pe.wait_ge(head_kept, before + MT1 + MT2)
                    for t in range(SUBS):
                        for g in range(MT2):
                            last = pe.matmul(bank[:, t:t + 1], h2_sb[:, g, t * P:(t + 1) * P], w3_sb[:, g:g + 1],
                                             start=g == 0, stop=g == MT2 - 1)
                last.then_inc(head_done, 1)

            pe.wait_ge(consts_loaded, 32)
            for q in range(HALVES * QUADS):
                for h, m in COUPLES_AT[q]:
                    transpose_couple(h, m)
                for b in range(QUAD * q, QUAD * (q + 1)):
                    bilinear(b)
                if q:
                    reduce_quad(q - 1)
                if q in HEAD_AT:
                    head(0, *HEAD_AT[q], head_ps[:, :])
            reduce_quad(HALVES * QUADS - 1)
            pe.wait_ge(duo_multiplied, HALVES * DUOS)
            for n in range(MT1):
                head(HALVES - 1, "l1", n, bil[n // 2][:, n % 2 * HB:(n % 2 + 1) * HB])
            for n in range(MT2):
                head(HALVES - 1, "l2", n, z_ps[n][:, :])
            head(HALVES - 1, "l3", 0, head_ps[:, :])



def kernel(**inputs):
    import concourse.bacc as bacc
    from concourse.bass_utils import run_bass_kernel_spmd

    get = {k: np.asarray(v) for k, v in inputs.items()}

    k = get["L0_rec_kernel"]
    k_blocks = np.zeros((EMBED, NBLK, 2, EMBED), k.dtype)
    for q, (j, m) in enumerate(BLOCKS):
        for s in range(2):
            if 2 * m + s < j:
                k_blocks[:, q, s] = k[:, pair_index(2 * m + s, j)]

    order = np.zeros((GROUPS, P), np.int64)
    for q, (j, m) in enumerate(BLOCKS):
        for s in range(2):
            i = 2 * m + s
            order[z_row(q, s)] = pair_index(i, j) if i < j else FIELDS * (FIELDS - 1) // 2 + LONE.index(q)

    selector = np.zeros((P, GROUP_QUADS, 32), np.float32)
    for n in range(GROUP_QUADS):
        for s in range(2):
            selector[s * EMBED:(s + 1) * EMBED, n, 2 * n + s] = 1.0

    dense = get["dense_ctx"].reshape(P, TILES, DENSE).transpose(2, 1, 0).reshape(DENSE, BATCH)
    arrays = {
        "ids": get["ids"],
        "dense_rows": dense,
        "k_blocks": k_blocks.reshape(EMBED, -1),
        "w1": get["W_top1"][order.ravel()],
        "b1": get["b_top1"].reshape(MT1, P).T,
        "w2": get["W_top2"],
        "b2": get["b_top2"].reshape(MT2, P).T,
        "w3": get["W_top3"].reshape(MT2, P).T,
        "ident": np.eye(P, dtype=np.float32),
        "selector": selector.reshape(P, -1),
    }
    arrays |= {f"tbl_{f}": get[f"tbl_{f}"] for f in range(FIELDS)}
    arrays = {f"in_{name}": np.ascontiguousarray(a) for name, a in arrays.items()}

    nc = bacc.Bacc("TRN2", target_bir_lowering=False, num_devices=1)
    aps = {name[3:]: nc.dram_tensor(name, a.shape, mybir.dt.from_np(a.dtype), kind="ExternalInput").ap()
           for name, a in arrays.items()}
    y = nc.dram_tensor("out_y", (BATCH, 1), F32, kind="ExternalOutput").ap()
    tables = [aps.pop(f"tbl_{f}") for f in range(FIELDS)]
    interaction_tower(nc, tables=tables, y=y, **aps)
    r = run_bass_kernel_spmd(nc, [arrays], core_ids=[0])
    return r.results[0]["out_y"]
```

```python
from contextlib import ExitStack

import numpy as np

import concourse.bass as bass
from concourse import mybir

F32 = mybir.dt.float32
F32R = mybir.dt.float32r
I32 = mybir.dt.int32
ALU = mybir.AluOpType
ACT = mybir.ActivationFunctionType

P = 128
BATCH, FIELDS, EMBED, DENSE = 1024, 32, 64, 16
HIDDEN1, HIDDEN2 = 512, 256
HALVES = 2
HB = BATCH // HALVES
SUBS = HB // P
TILES = BATCH // P
COUPLES = FIELDS // 2

BLOCKS = [(j, m) for j in range(1, FIELDS) for m in range((j + 1) // 2)]
NBLK = len(BLOCKS)
QUAD = 4
QUADS = NBLK // QUAD
DUOS = NBLK // 2
GROUP_QUADS = P // (2 * QUAD)
GROUPS = QUADS // GROUP_QUADS
CHUNK_QUADS = 4
CHUNKS = QUADS // CHUNK_QUADS
MT1, MT2 = HIDDEN1 // P, HIDDEN2 // P

K_RING, S_RING, E_RING, G_RING, Y_RING, B_RING = 3, 6, 4, 8, 4, 3
HI_AHEAD, LO_AHEAD, LOAD_AHEAD = 3, 2, 7


def pair_index(i, j):
    return i * (2 * FIELDS - i - 1) // 2 + j - i - 1


def z_row(q, s):
    g, r = divmod(q, GROUP_QUADS * QUAD)
    return g, 32 * (r % QUAD) + 2 * (r // QUAD) + s


LONE = [q for q, (j, m) in enumerate(BLOCKS) if 2 * m + 1 == j]
FIRST_BLOCK = [next(q for q, (j, _) in enumerate(BLOCKS) if j // 2 == m) for m in range(COUPLES)]
END_BLOCK = FIRST_BLOCK[1:] + [NBLK]


EARLY0 = {m: 0 for m in range(6)}
EARLY1 = {0: 9, 1: 6, 2: 5, 3: 3, 4: 4, 5: 4, 6: 4, 7: 4}


def couple_quad(h, m):
    need = h * QUADS + FIRST_BLOCK[m] // QUAD
    ahead = (EARLY0 if h == 0 else EARLY1).get(m, 3)
    return max(need - ahead, 0)


COUPLES_AT = [[] for _ in range(HALVES * QUADS)]
for _h in range(HALVES):
    for _m in range(COUPLES):
        COUPLES_AT[couple_quad(_h, _m)].append((_h, _m))


def direct(h, m):
    return h == 0 and m in EARLY0


def moved_count(n):
    return sum(not direct(*divmod(k, COUPLES)) for k in range(n % E_RING, n + 1, E_RING))


SHARE_FROM, SHARE_TO, SHARE_AGAIN, ALL_FROM, SHARE_EVERY = 16, 70, 84, 96, 3
GATHER_FROM, GATHER_EVERY, GATHER_EVERY_LATE = 20, 3.75, 2.5
GATHERED_FIRST = 11


def lo_by_pool(q):
    return q >= ALL_FROM or (SHARE_FROM <= q < SHARE_TO or SHARE_AGAIN <= q) and q % SHARE_EVERY == 0


def lo_count(q, pool):
    return sum(lo_by_pool(n) == pool for n in range(q + 1))


def gather_quad(n):
    if n < GATHERED_FIRST:
        return 0
    pace = int(GATHER_FROM + GATHER_EVERY * (n - GATHERED_FIRST))
    if pace > SHARE_TO:
        pace = int(SHARE_TO + (pace - SHARE_TO) * GATHER_EVERY_LATE / GATHER_EVERY)
    return max(pace, couple_quad(*divmod(n - G_RING, COUPLES)) + 1)


GATHERS_AT = [[n for n in range(HALVES * COUPLES) if gather_quad(n) == q] for q in range(HALVES * QUADS)]

HEAD_QUADS = [2, 3, 4, 5, 7, 8, 10]
HEAD_KINDS = [("l1", n) for n in range(MT1)] + [("l2", n) for n in range(MT2)] + [("l3", 0)]
HEAD_AT = {QUADS + at: piece for at, piece in zip(HEAD_QUADS, HEAD_KINDS)}
HEAD_STEPS = MT1 + MT2 + 1


def couples_before(q):
    return sum(len(couples) for couples in COUPLES_AT[:q + 1])


def head_pieces_before(q):
    return sum(at < q for at in HEAD_AT)


def interaction_tower(nc, ids, tables, dense_rows, k_blocks, w1, b1, w2, b2, w3, ident, selector, y):
    ctx = ExitStack()
    with ctx:
        def sb(name, shape, dt=F32):
            return ctx.enter_context(nc.sbuf_tensor(name, shape, dt))

        def pb(name, shape):
            return ctx.enter_context(nc.psum_tensor(name, shape, F32))

        def sem(name):
            return ctx.enter_context(nc.semaphore(name))

        ids_sb = sb("ids_sb", [P, TILES, FIELDS], I32)
        ident_sb = sb("ident_sb", [P, P])
        sel_sb = sb("sel_sb", [P, GROUP_QUADS, 32])
        b1_sb = sb("b1_sb", [P, MT1])
        b2_sb = sb("b2_sb", [P, MT2])
        w1_sb = sb("w1_sb", [P, GROUPS, HIDDEN1])
        w2_sb = sb("w2_sb", [P, MT1, HIDDEN2])
        w3_sb = sb("w3_sb", [P, MT2])
        gathered = sb("gathered", [P, G_RING, SUBS, P])
        k_raw = sb("k_raw", [P, K_RING, CHUNK_QUADS, QUAD * P])
        k_hi = sb("k_hi", [P, S_RING, QUAD * P], F32R)
        k_lo = sb("k_lo", [P, S_RING, QUAD * P], F32R)
        emb = sb("emb", [P, HALVES, COUPLES, HB])
        split = sb("split", [P, E_RING, 2, HB], F32R)
        couple_hi = sb("couple_hi", [P, 2, HB], F32R)
        couple_lo = sb("couple_lo", [P, 2, HB], F32R)
        prod = sb("prod", [P, Y_RING, 2 * HB])
        z_sb = sb("z_sb", [P, GROUPS, HB])
        h1_sb = sb("h1_sb", [P, MT1, HB])
        h2_sb = sb("h2_sb", [P, MT2, HB])
        y_sb = sb("y_sb", [P, TILES])

        bil = [pb(f"bil{i}", [P, 2 * HB]) for i in range(B_RING)]
        z_ps = pb("z_ps", [P, HB])
        side_ps = pb("side_ps", [P, HB])

        ids_loaded = sem("ids_loaded")
        consts_loaded = sem("consts_loaded")
        head_loaded = sem("head_loaded")
        couple_gathered = [sem(f"couple_gathered{i}") for i in range(G_RING)]
        k_loaded = [sem(f"k_loaded{i}") for i in range(K_RING)]
        couple_transposed = sem("couple_transposed")
        emb_kept = sem("emb_kept")
        emb_hi = sem("emb_hi")
        emb_lo = sem("emb_lo")
        emb_moved = [sem(f"emb_moved{i}") for i in range(E_RING)]
        k_hi_ready = sem("k_hi_ready")
        k_lo_by_dve = sem("k_lo_by_dve")
        k_lo_by_pool = sem("k_lo_by_pool")
        block_done = sem("block_done")
        duo_multiplied = sem("duo_multiplied")
        quad_reduced = sem("quad_reduced")
        z_copied = sem("z_copied")
        dense_placed = [sem(f"dense_placed{g}") for g in range(GROUPS)]
        head_done = sem("head_done")
        head_kept = sem("head_kept")
        y_stored = sem("y_stored")

        def rows_placed(h, g):
            return 16 * (h + 1) * sum(z_row(q, 1)[0] == g for q in LONE)

        def wait_lo(engine, q):
            if lo_by_pool(q):
                engine.wait_ge(k_lo_by_pool, lo_count(q, True))
            else:
                engine.wait_ge(k_lo_by_dve, lo_count(q, False))

        block = ctx.enter_context(nc.Block())

        @block.sync
        def _(sp):
            sp.dma_start(ids_sb[:, :, :], ids.rearrange("(p t) f -> p t f", p=P)).then_inc(ids_loaded, 16)

            def load_chunk(n):
                if n >= K_RING:
                    last = (n - K_RING + 1) * CHUNK_QUADS - 1
                    sp.wait_ge(k_hi_ready, last + 1)
                    sp.wait_ge(k_lo_by_dve, lo_count(last, False))
                    if lo_count(last, True):
                        sp.wait_ge(k_lo_by_pool, lo_count(last, True))
                c = n % CHUNKS
                src = k_blocks[:, c * CHUNK_QUADS * QUAD * P:(c + 1) * CHUNK_QUADS * QUAD * P]
                for d in range(2):
                    dst = k_raw[d * EMBED:(d + 1) * EMBED, n % K_RING, :, :].rearrange("p q n -> p (q n)")
                    sp.dma_start(dst, src).then_inc(k_loaded[n % K_RING], 16)

            def move_lo(h, m):
                n = h * COUPLES + m
                sp.wait_ge(emb_lo, n + 1)
                sp.dma_start(split[EMBED:P, n % E_RING, 0, :].bitcast(F32), couple_lo[0:EMBED, n % 2, :].bitcast(F32))\
                  .then_inc(emb_moved[n % E_RING], 16)
                sp.dma_start(split[0:EMBED, n % E_RING, 1, :].bitcast(F32), couple_lo[EMBED:P, n % 2, :].bitcast(F32))\
                  .then_inc(emb_moved[n % E_RING], 16)

            def place_dense(group):
                h, g = divmod(group, GROUPS)
                sp.wait_ge(z_copied, group + 1)
                for f, q in enumerate(LONE):
                    zg, row = z_row(q, 1)
                    if zg == g:
                        sp.dma_start(z_sb[row:row + 1, g, :], dense_rows[f:f + 1, h * HB:(h + 1) * HB])\
                          .then_inc(dense_placed[g], 16)

            load_chunk(0)
            sp.dma_start(ident_sb[:, :], ident).then_inc(consts_loaded, 16)
            sp.dma_start(sel_sb[:, :, :], selector.rearrange("p (k c) -> p k c", c=32)).then_inc(consts_loaded, 16)
            load_chunk(1)
            load_chunk(2)
            sp.dma_start(w1_sb[:, :, :], w1.rearrange("(g p) n -> p g n", p=P)).then_inc(head_loaded, 16)
            sp.dma_start(w2_sb[:, :, :], w2.rearrange("(g p) n -> p g n", p=P)).then_inc(head_loaded, 16)
            sp.dma_start(w3_sb[:, :], w3).then_inc(head_loaded, 16)
            sp.dma_start(b1_sb[:, :], b1).then_inc(head_loaded, 16)
            sp.dma_start(b2_sb[:, :], b2).then_inc(head_loaded, 16)
            for q in range(HALVES * QUADS):
                for h, m in COUPLES_AT[q]:
                    if not direct(h, m):
                        move_lo(h, m)
                if q > GROUP_QUADS and q % GROUP_QUADS == 1:
                    place_dense(q // GROUP_QUADS - 1)
                n, at = divmod(q + LOAD_AHEAD, CHUNK_QUADS)
                if at == 0 and K_RING <= n < HALVES * CHUNKS:
                    load_chunk(n)
            place_dense(HALVES * GROUPS - 1)
            sp.wait_ge(head_kept, HALVES * HEAD_STEPS)
            sp.dma_start(y.rearrange("(p t) o -> p (t o)", p=P), y_sb[:, :]).then_inc(y_stored, 16)
            sp.wait_ge(y_stored, 16)

        @block.gpsimd
        def _(pool):
            def gather_couple(n):
                h, m = divmod(n, COUPLES)
                if n >= G_RING:
                    pool.wait_ge(couple_transposed, n - G_RING + 1)
                for s in range(2):
                    for t in range(SUBS):
                        f = 2 * m + s
                        pool.indirect_dma_start(
                            gathered[:, n % G_RING, t, s * EMBED:(s + 1) * EMBED], None, tables[f],
                            bass.IndirectOffsetOnAxis(ap=ids_sb[:, h * SUBS + t, f:f + 1], axis=0),
                        ).then_inc(couple_gathered[n % G_RING], 16)

            def split_lo(q):
                chunk = q // CHUNK_QUADS
                pool.wait_ge(k_hi_ready, q + 1)
                pool.tensor_tensor(k_lo[:, q % S_RING, :], k_raw[:, chunk % K_RING, q % CHUNK_QUADS, :],
                                   k_hi[:, q % S_RING, :].bitcast(F32), ALU.subtract).then_inc(k_lo_by_pool, 1)

            pool.wait_ge(ids_loaded, 16)
            for q in range(HALVES * QUADS):
                for n in GATHERS_AT[q]:
                    gather_couple(n)
                if q + LO_AHEAD < HALVES * QUADS and lo_by_pool(q + LO_AHEAD):
                    split_lo(q + LO_AHEAD)

        @block.scalar
        def _(act):
            def split_hi(q):
                chunk = q // CHUNK_QUADS
                act.wait_ge(k_loaded[chunk % K_RING], 32 * (chunk // K_RING + 1))
                if q >= S_RING:
                    act.wait_ge(block_done, QUAD * (q - S_RING + 1))
                act.activation(k_hi[:, q % S_RING, :], k_raw[:, chunk % K_RING, q % CHUNK_QUADS, :], ACT.Copy)\
                   .then_inc(k_hi_ready, 1)

            def keep_couple(h, m):
                n = h * COUPLES + m
                act.wait_ge(couple_transposed, n + 1)
                if n >= E_RING:
                    ph, pm = divmod(n - E_RING, COUPLES)
                    act.wait_ge(block_done, ph * NBLK + END_BLOCK[pm])
                if direct(h, m):
                    act.activation(emb[:, h, m, :], side_ps[:, :], ACT.Copy).then_inc(emb_kept, 1)
                else:
                    act.activation(emb[:, h, m, :], side_ps[:, :], ACT.Copy)
                    act.wait_ge(emb_lo, n - 1)
                    act.activation(couple_hi[:, n % 2, :], side_ps[:, :], ACT.Copy).then_inc(emb_kept, 1)
                act.activation(split[0:EMBED, n % E_RING, 0, :], side_ps[0:EMBED, :], ACT.Copy)
                last = act.activation(split[EMBED:P, n % E_RING, 1, :], side_ps[EMBED:P, :], ACT.Copy)
                last.then_inc(emb_hi, 1)

            def copy_z(group):
                act.wait_ge(quad_reduced, (group + 1) * GROUP_QUADS)
                if group >= GROUPS:
                    act.wait_ge(head_done, (group // GROUPS - 1) * HEAD_STEPS + MT1)
                act.activation(z_sb[:, group % GROUPS, :], z_ps[:, :], ACT.Copy).then_inc(z_copied, 1)

            def keep_head(h, kind, n, bank):
                step = {"l1": n, "l2": MT1 + n, "l3": MT1 + MT2}[kind]
                act.wait_ge(head_done, h * HEAD_STEPS + step + 1)
                if kind == "l1":
                    act.activation(h1_sb[:, n, :], bank, ACT.Relu, bias=b1_sb[:, n:n + 1]).then_inc(head_kept, 1)
                elif kind == "l2":
                    act.activation(h2_sb[:, n, :], bank, ACT.Relu, bias=b2_sb[:, n:n + 1]).then_inc(head_kept, 1)
                else:
                    act.activation(y_sb[:, h * SUBS:(h + 1) * SUBS], bank[:, 0:SUBS], ACT.Copy).then_inc(head_kept, 1)

            act.wait_ge(head_loaded, 16 * 5)
            for q in range(HI_AHEAD):
                split_hi(q)
            for q in range(HALVES * QUADS):
                for h, m in COUPLES_AT[q]:
                    keep_couple(h, m)
                if q + HI_AHEAD < HALVES * QUADS:
                    split_hi(q + HI_AHEAD)
                if q and q % GROUP_QUADS == 0:
                    copy_z(q // GROUP_QUADS - 1)
                if q in HEAD_AT:
                    keep_head(0, *HEAD_AT[q], side_ps[:, :])
            copy_z(HALVES * GROUPS - 1)
            for n in range(MT1):
                keep_head(HALVES - 1, "l1", n, bil[n // 2][:, n % 2 * HB:(n % 2 + 1) * HB])
            for n in range(MT2):
                keep_head(HALVES - 1, "l2", n, bil[2][:, n * HB:(n + 1) * HB])
            keep_head(HALVES - 1, "l3", 0, side_ps[:, :])

        @block.vector
        def _(dve):
            def split_lo(q):
                chunk = q // CHUNK_QUADS
                dve.wait_ge(k_hi_ready, q + 1)
                dve.tensor_tensor(k_lo[:, q % S_RING, :], k_raw[:, chunk % K_RING, q % CHUNK_QUADS, :],
                                  k_hi[:, q % S_RING, :].bitcast(F32), ALU.subtract).then_inc(k_lo_by_dve, 1)

            def split_couple(h, m):
                n = h * COUPLES + m
                if not direct(h, m):
                    dve.wait_ge(emb_kept, n + 1)
                    if moved_count(n - 2):
                        dve.wait_ge(emb_moved[(n - 2) % E_RING], 32 * moved_count(n - 2))
                    dve.tensor_tensor(couple_lo[:, n % 2, :], emb[:, h, m, :],
                                      couple_hi[:, n % 2, :].bitcast(F32), ALU.subtract).then_inc(emb_lo, 1)
                    return
                dve.wait_ge(emb_hi, n + 1)
                dve.tensor_tensor(split[EMBED:P, n % E_RING, 0, :], emb[0:EMBED, h, m, :],
                                  split[0:EMBED, n % E_RING, 0, :].bitcast(F32), ALU.subtract)
                dve.tensor_tensor(split[0:EMBED, n % E_RING, 1, :], emb[EMBED:P, h, m, :],
                                  split[EMBED:P, n % E_RING, 1, :].bitcast(F32), ALU.subtract).then_inc(emb_lo, 1)

            def multiply(d):
                h, first = divmod(2 * d, NBLK)
                ma, mb = BLOCKS[first][1], BLOCKS[first + 1][1]
                dve.wait_ge(block_done, 2 * d + 2)
                if d >= Y_RING:
                    dve.wait_ge(quad_reduced, (d - Y_RING) // 2 + 1)
                dve.wait_ge(emb_kept, h * COUPLES + max(BLOCKS[first][0], BLOCKS[first + 1][0]) // 2 + 1)
                out = prod[:, d % Y_RING, :]
                if mb > ma:
                    dve.tensor_tensor(out.rearrange("p (b n) -> p b n", b=2),
                                      bil[d % B_RING][:, :].rearrange("p (b n) -> p b n", b=2),
                                      emb[:, h, ma:mb + 1:mb - ma, :], ALU.mult).then_inc(duo_multiplied, 1)
                else:
                    dve.tensor_tensor(out[:, 0:HB], bil[d % B_RING][:, 0:HB], emb[:, h, ma, :], ALU.mult)
                    dve.tensor_tensor(out[:, HB:2 * HB], bil[d % B_RING][:, HB:2 * HB], emb[:, h, mb, :], ALU.mult)\
                       .then_inc(duo_multiplied, 1)

            for q in range(LO_AHEAD):
                split_lo(q)
            for q in range(HALVES * QUADS):
                for h, m in COUPLES_AT[q]:
                    if h == 0 and m < 6:
                        split_couple(h, m)
                multiply(2 * q)
                if q + LO_AHEAD < HALVES * QUADS and not lo_by_pool(q + LO_AHEAD):
                    split_lo(q + LO_AHEAD)
                multiply(2 * q + 1)
                for h, m in COUPLES_AT[q]:
                    if h > 0 or m >= 6:
                        split_couple(h, m)

        @block.tensor
        def _(pe):
            def transpose_couple(q, h, m):
                n = h * COUPLES + m
                pe.wait_ge(couple_gathered[n % G_RING], 16 * 2 * SUBS * (n // G_RING + 1))
                if n:
                    pe.wait_ge(emb_hi, n)
                if head_pieces_before(q):
                    pe.wait_ge(head_kept, head_pieces_before(q))
                for t in range(SUBS):
                    last = pe.transpose(side_ps[:, t * P:(t + 1) * P], gathered[:, n % G_RING, t, :], ident_sb[:, :])
                last.then_inc(couple_transposed, 1)

            def bilinear(b):
                h, q = divmod(b, NBLK)
                j, _ = BLOCKS[q]
                n = h * COUPLES + j // 2
                quad, at = divmod(b, QUAD)
                if at == 0:
                    wait_lo(pe, quad)
                if q == 0 or BLOCKS[q - 1][0] // 2 != j // 2:
                    if direct(h, j // 2):
                        pe.wait_ge(emb_lo, n + 1)
                    else:
                        pe.wait_ge(emb_hi, n + 1)
                        pe.wait_ge(emb_moved[n % E_RING], 32 * moved_count(n))
                if b % 2 == 0 and b >= 2 * B_RING:
                    pe.wait_ge(duo_multiplied, b // 2 - B_RING + 1)
                out = bil[b // 2 % B_RING][:, b % 2 * HB:(b % 2 + 1) * HB]
                moving = split[:, n % E_RING, j % 2, :]
                cols = slice(at * P, (at + 1) * P)
                pe.matmul(out, k_hi[:, quad % S_RING, cols], moving, start=True, stop=False)
                pe.matmul(out, k_lo[:, quad % S_RING, cols], moving, start=False, stop=True).then_inc(block_done, 1)

            def reduce_quad(q):
                group, k = divmod(q, GROUP_QUADS)
                pe.wait_ge(duo_multiplied, 2 * q + 2)
                if k == 0 and group:
                    pe.wait_ge(z_copied, group)
                for c in range(QUAD):
                    d = 2 * q + c // 2
                    last = pe.matmul(z_ps[32 * c:32 * (c + 1), :], sel_sb[:, k, :],
                                     prod[:, d % Y_RING, c % 2 * HB:(c % 2 + 1) * HB],
                                     start=k == 0, stop=k == GROUP_QUADS - 1, tile_position=(0, 32 * c))
                last.then_inc(quad_reduced, 1)

            def head(h, kind, n, bank):
                before = h * HEAD_STEPS
                if kind == "l1":
                    pe.wait_ge(head_kept, before + n)
                    for g in range(GROUPS):
                        pe.wait_ge(z_copied, h * GROUPS + g + 1)
                        pe.wait_ge(dense_placed[g], rows_placed(h, g))
                        last = pe.matmul(bank, w1_sb[:, g, n * P:(n + 1) * P], z_sb[:, g, :],
                                         start=g == 0, stop=g == GROUPS - 1)
                elif kind == "l2":
                    if h == 0:
                        pe.wait_ge(head_kept, before + MT1 + n)
                    for g in range(MT1):
                        pe.wait_ge(head_kept, before + g + 1)
                        last = pe.matmul(bank, w2_sb[:, g, n * P:(n + 1) * P], h1_sb[:, g, :],
                                         start=g == 0, stop=g == MT1 - 1)
                else:
                    pe.wait_ge(head_kept, before + MT1 + MT2)
                    for t in range(SUBS):
                        for g in range(MT2):
                            last = pe.matmul(bank[:, t:t + 1], h2_sb[:, g, t * P:(t + 1) * P], w3_sb[:, g:g + 1],
                                             start=g == 0, stop=g == MT2 - 1)
                last.then_inc(head_done, 1)

            pe.wait_ge(consts_loaded, 32)
            for q in range(HALVES * QUADS):
                for h, m in COUPLES_AT[q]:
                    transpose_couple(q, h, m)
                for b in range(QUAD * q, QUAD * (q + 1)):
                    bilinear(b)
                if q:
                    reduce_quad(q - 1)
                if q in HEAD_AT:
                    pe.wait_ge(emb_hi, couples_before(q))
                    head(0, *HEAD_AT[q], side_ps[:, :])
            reduce_quad(HALVES * QUADS - 1)
            pe.wait_ge(duo_multiplied, HALVES * DUOS)
            for g in range(GROUPS):
                pe.wait_ge(z_copied, (HALVES - 1) * GROUPS + g + 1)
                pe.wait_ge(dense_placed[g], rows_placed(HALVES - 1, g))
                for n in range(MT1):
                    last = pe.matmul(bil[n // 2][:, n % 2 * HB:(n % 2 + 1) * HB], w1_sb[:, g, n * P:(n + 1) * P],
                                     z_sb[:, g, :], start=g == 0, stop=g == GROUPS - 1)
                    if g == GROUPS - 1:
                        last.then_inc(head_done, 1)
            for n in range(MT2):
                head(HALVES - 1, "l2", n, bil[2][:, n * HB:(n + 1) * HB])
            head(HALVES - 1, "l3", 0, side_ps[:, :])



def kernel(**inputs):
    import concourse.bacc as bacc
    from concourse.bass_utils import run_bass_kernel_spmd

    get = {k: np.asarray(v) for k, v in inputs.items()}

    k = get["L0_rec_kernel"]
    k_blocks = np.zeros((EMBED, NBLK, 2, EMBED), k.dtype)
    for q, (j, m) in enumerate(BLOCKS):
        for s in range(2):
            if 2 * m + s < j:
                k_blocks[:, q, s] = k[:, pair_index(2 * m + s, j)]

    order = np.zeros((GROUPS, P), np.int64)
    for q, (j, m) in enumerate(BLOCKS):
        for s in range(2):
            i = 2 * m + s
            order[z_row(q, s)] = pair_index(i, j) if i < j else FIELDS * (FIELDS - 1) // 2 + LONE.index(q)

    selector = np.zeros((P, GROUP_QUADS, 32), np.float32)
    for n in range(GROUP_QUADS):
        for s in range(2):
            selector[s * EMBED:(s + 1) * EMBED, n, 2 * n + s] = 1.0

    dense = get["dense_ctx"].reshape(P, TILES, DENSE).transpose(2, 1, 0).reshape(DENSE, BATCH)
    arrays = {
        "ids": get["ids"],
        "dense_rows": dense,
        "k_blocks": k_blocks.reshape(EMBED, -1),
        "w1": get["W_top1"][order.ravel()],
        "b1": get["b_top1"].reshape(MT1, P).T,
        "w2": get["W_top2"],
        "b2": get["b_top2"].reshape(MT2, P).T,
        "w3": get["W_top3"].reshape(MT2, P).T,
        "ident": np.eye(P, dtype=np.float32),
        "selector": selector.reshape(P, -1),
    }
    arrays |= {f"tbl_{f}": get[f"tbl_{f}"] for f in range(FIELDS)}
    arrays = {f"in_{name}": np.ascontiguousarray(a) for name, a in arrays.items()}

    nc = bacc.Bacc("TRN2", target_bir_lowering=False, num_devices=1)
    aps = {name[3:]: nc.dram_tensor(name, a.shape, mybir.dt.from_np(a.dtype), kind="ExternalInput").ap()
           for name, a in arrays.items()}
    y = nc.dram_tensor("out_y", (BATCH, 1), F32, kind="ExternalOutput").ap()
    tables = [aps.pop(f"tbl_{f}") for f in range(FIELDS)]
    interaction_tower(nc, tables=tables, y=y, **aps)
    r = run_bass_kernel_spmd(nc, [arrays], core_ids=[0])
    return r.results[0]["out_y"]
```

```python
from contextlib import ExitStack
from functools import cache

import numpy as np

import concourse.bass as bass
from concourse import mybir

F32 = mybir.dt.float32
F32R = mybir.dt.float32r
I32 = mybir.dt.int32
ALU = mybir.AluOpType
ACT = mybir.ActivationFunctionType

P = 128
BATCH, FIELDS, EMBED, DENSE = 1024, 32, 64, 16
HIDDEN1, HIDDEN2 = 512, 256
HALVES = 2
HB = BATCH // HALVES
SUBS = HB // P
TILES = BATCH // P
COUPLES = FIELDS // 2
NCOUPLE = HALVES * COUPLES
MIXED = 2


def block_list():
    blocks = []
    for m in range(COUPLES):
        even, odd = 2 * m, 2 * m + 1
        whole = m - m % 2
        blocks += [(even, 2 * c, 2 * c + 1, c, m) for c in range(whole)]
        if m % 2:
            blocks.append((even, even - 2, odd - 2, m - 1, m))
            blocks.append((even - 2, odd, odd - 2, COUPLES + 1, m))
        blocks += [(odd, 2 * c, 2 * c + 1, c, m) for c in range(whole)]
        if m % 2:
            blocks.append((odd, even, odd - 2, COUPLES, m))
    return blocks


BLOCKS = block_list()
NBLK = len(BLOCKS)
QUAD = 4
QUADS = NBLK // QUAD
NPASS = HALVES * QUADS
GROUP_QUADS = P // (2 * QUAD)
GROUPS = -(-QUADS // GROUP_QUADS)
SEL_WIDTH = 2 * GROUP_QUADS - 2 + 32
MT1, MT2 = HIDDEN1 // P, HIDDEN2 // P

K_RING, S_RING, E_RING, G_RING, Y_RING, B_RING = 3, 5, 5, 4, 6, 3
LOAD_AHEAD, HI_AHEAD, LO_AHEAD = 6, 3, 2
REDUCED = 2
CHUNK_QUADS = 3

LOADS = [(h * QUADS + first, min(CHUNK_QUADS, QUADS - first)) for h in range(HALVES)
         for first in range(0, QUADS, CHUNK_QUADS)]
LOAD_OF = [(n, x - first) for n, (first, count) in enumerate(LOADS) for x in range(first, first + count)]

NEEDED = [next((b for b, block in enumerate(BLOCKS) if block[4] == m), 0) for m in range(COUPLES)]
NEEDED_TO = [max(b for b, block in enumerate(BLOCKS) if block[0] // 2 == m) + 1 for m in range(COUPLES)]

DIRECT = 5
GATHERED_FIRST, GATHER_FROM, GATHER_EVERY = 11, 17, (3.75, 3.75)
TRANSPOSE_AFTER = 5
SPLIT_AHEAD, SPLIT_APART = 3, 2


@cache
def split_wish(n):
    h, m = divmod(n, COUPLES)
    at = h * QUADS + NEEDED[m] // QUAD - (0 if n < DIRECT else SPLIT_AHEAD)
    return min(at, split_wish(n + 1) - SPLIT_APART) if GATHERED_FIRST <= n < NCOUPLE - 1 else at


@cache
def split_pass(n):
    at = [split_wish(n), split_pass(n - 1) if n else 0]
    if n >= E_RING:
        ph, pm = divmod(n - E_RING, COUPLES)
        at.append((ph * NBLK + NEEDED_TO[pm] - 1) // QUAD + 1)
    return max(at)


POOL_SHARE = [(0, 0), (17, 5), (18, 3), (56, 4), (96, 6), (104, 9)]


def gather_pass(n):
    late = max(n - COUPLES, 0)
    pace = int(GATHER_FROM + GATHER_EVERY[0] * (n - late - GATHERED_FIRST) + GATHER_EVERY[1] * late)
    return max(pace if n >= GATHERED_FIRST else 0, transpose_pass(n - G_RING) + 1 if n >= G_RING else 0)


@cache
def transpose_pass(n):
    return max(min(gather_pass(n) + TRANSPOSE_AFTER, split_pass(n)) if n >= GATHERED_FIRST else split_pass(n),
               transpose_pass(n - 1) if n else 0)


GATHERED_AT, TRANSPOSED_AT, SPLIT_AT = ([[n for n in range(NCOUPLE) if at(n) == x] for x in range(NPASS)]
                                        for at in (gather_pass, transpose_pass, split_pass))

MIXES = [(h, m) for h in range(HALVES) for m in range(1, COUPLES, 2)]
MIX_AHEAD = 3


def mixed_done(h, m):
    return h * NBLK + NEEDED[m - 1] if m > 1 else 0


def mix_pass(h, m):
    first = next(b for b, block in enumerate(BLOCKS) if block[3] >= COUPLES and block[4] == m)
    at = [h * QUADS + first // QUAD - MIX_AHEAD, transpose_pass(h * COUPLES + m)]
    if mixed_done(h, m):
        at.append((mixed_done(h, m) - 1) // QUAD + 1)
    return max(at)


def moved_count(n):
    return sum(k >= DIRECT for k in range(n % E_RING, n + 1, E_RING))


def lo_by_pool(x):
    share = [s for first, s in POOL_SHARE if first <= x][-1]
    return (x + 1) * share // 10 > x * share // 10


def lo_count(x, pool):
    return sum(lo_by_pool(k) == pool for k in range(x + 1))


def prepared_at(x, ahead):
    return range(0 if x == 0 else x + ahead, min(x + ahead + 1, NPASS))


FILLED = [(h * QUADS + min(GROUP_QUADS * (g + 1), QUADS) - 1, h, g) for h in range(HALVES) for g in range(GROUPS)]


def pair_index(i, j):
    return i * (2 * FIELDS - i - 1) // 2 + j - i - 1


def z_row(b, s):
    g, r = divmod(b, GROUP_QUADS * QUAD)
    return g, 32 * (r % QUAD) + 2 * (r // QUAD) + s


FREE_ROWS = [(GROUPS - 1, 32 * c + 2 * (QUADS % GROUP_QUADS), 32 - 2 * (QUADS % GROUP_QUADS)) for c in range(QUAD)]

PIECES = [("l1", n) for n in range(MT1)] + [("l2", n) for n in range(MT2)] + [("l3", 0)]
HEAD_PASSES = [6, 8, 10, 12, 14, 16, 18]
HEAD_AT = {QUADS + at: i for i, at in enumerate(HEAD_PASSES)}


def interaction_tower(nc, ids, tables, dense_rows, k_blocks, w1, b1, w2, b2, w3, ident, selector, y):
    ctx = ExitStack()
    with ctx:
        def sb(name, shape, dt=F32):
            return ctx.enter_context(nc.sbuf_tensor(name, shape, dt))

        def pb(name, shape):
            return ctx.enter_context(nc.psum_tensor(name, shape, F32))

        def sem(name):
            return ctx.enter_context(nc.semaphore(name))

        ids_sb = sb("ids_sb", [P, TILES, FIELDS], I32)
        ident_sb = sb("ident_sb", [P, P])
        sel_sb = sb("sel_sb", [P, SEL_WIDTH])
        b1_sb = sb("b1_sb", [P, MT1])
        b2_sb = sb("b2_sb", [P, MT2])
        w1_sb = sb("w1_sb", [P, GROUPS, HIDDEN1])
        w2_sb = sb("w2_sb", [P, MT1, HIDDEN2])
        w3_sb = sb("w3_sb", [P, MT2])
        gathered = sb("gathered", [P, G_RING, SUBS, P])
        k_raw = sb("k_raw", [P, K_RING, CHUNK_QUADS, QUAD * P])
        k_hi = sb("k_hi", [P, S_RING, QUAD * P], F32R)
        k_lo = sb("k_lo", [P, S_RING, QUAD * P], F32R)
        emb = sb("emb", [P, HALVES, COUPLES + MIXED, HB])
        split = sb("split", [P, E_RING, 2, HB], F32R)
        couple_hi = sb("couple_hi", [P, 2, HB], F32R)
        couple_lo = sb("couple_lo", [P, 2, HB], F32R)
        prod = sb("prod", [P, Y_RING, 2, HB])
        z_sb = sb("z_sb", [P, GROUPS, HB])
        h1_sb = sb("h1_sb", [P, MT1, HB])
        h2_sb = sb("h2_sb", [P, MT2, HB])
        y_sb = sb("y_sb", [P, TILES])

        bil = [pb(f"bil{i}", [P, 2, HB]) for i in range(B_RING)]
        z_ps = pb("z_ps", [P, HB])
        side_ps = pb("side_ps", [P, HB])
        bil_banks = [bil[i // 2][:, i % 2, :] for i in range(2 * B_RING)]

        ids_loaded = sem("ids_loaded")
        consts_loaded = sem("consts_loaded")
        head_loaded = sem("head_loaded")
        couple_gathered = [sem(f"couple_gathered{i}") for i in range(G_RING)]
        k_loaded = [sem(f"k_loaded{i}") for i in range(K_RING)]
        couple_transposed = sem("couple_transposed")
        emb_kept = sem("emb_kept")
        couple_hi_ready = sem("couple_hi_ready")
        emb_hi = sem("emb_hi")
        mixed_kept = sem("mixed_kept")
        emb_lo = sem("emb_lo")
        emb_moved = [sem(f"emb_moved{i}") for i in range(E_RING)]
        k_hi_ready = sem("k_hi_ready")
        k_lo_by_dve = sem("k_lo_by_dve")
        k_lo_by_pool = sem("k_lo_by_pool")
        block_done = sem("block_done")
        duo_multiplied = sem("duo_multiplied")
        pass_reduced = sem("pass_reduced")
        z_copied = sem("z_copied")
        dense_placed = sem("dense_placed")
        head_done = sem("head_done")
        head_kept = sem("head_kept")
        y_stored = sem("y_stored")

        block = ctx.enter_context(nc.Block())

        @block.sync
        def _(sp):
            sp.dma_start(ids_sb[:, :, :], ids.rearrange("(p t) f -> p t f", p=P)).then_inc(ids_loaded, 16)

            def load_weights(n):
                if n >= K_RING:
                    last = sum(LOADS[n - K_RING]) - 1
                    sp.wait_ge(k_hi_ready, last + 1)
                    sp.wait_ge(k_lo_by_dve, lo_count(last, False))
                    if lo_count(last, True):
                        sp.wait_ge(k_lo_by_pool, lo_count(last, True))
                first, count = LOADS[n]
                width = QUAD * P
                src = k_blocks[:, first % QUADS * width:(first % QUADS + count) * width]
                for d in range(2):
                    dst = k_raw[d * EMBED:(d + 1) * EMBED, n % K_RING, 0:count, :].rearrange("p q n -> p (q n)")
                    sp.dma_start(dst, src).then_inc(k_loaded[n % K_RING], 16)

            def move_lo(n):
                sp.wait_ge(emb_lo, n + 1)
                sp.dma_start(split[EMBED:P, n % E_RING, 0, :].bitcast(F32), couple_lo[0:EMBED, n % 2, :].bitcast(F32))\
                  .then_inc(emb_moved[n % E_RING], 16)
                sp.dma_start(split[0:EMBED, n % E_RING, 1, :].bitcast(F32), couple_lo[EMBED:P, n % 2, :].bitcast(F32))\
                  .then_inc(emb_moved[n % E_RING], 16)

            def place_dense(h):
                sp.wait_ge(z_copied, (h + 1) * GROUPS)
                f = 0
                for g, row, rows in FREE_ROWS:
                    sp.dma_start(z_sb[row:row + rows, g, :], dense_rows[f:f + rows, h * HB:(h + 1) * HB])\
                      .then_inc(dense_placed, 16)
                    f += rows

            load_weights(0)
            sp.dma_start(ident_sb[:, :], ident).then_inc(consts_loaded, 16)
            sp.dma_start(sel_sb[:, :], selector).then_inc(consts_loaded, 16)
            load_weights(1)
            load_weights(2)
            sp.dma_start(w1_sb[:, :, :], w1.rearrange("(g p) n -> p g n", p=P)).then_inc(head_loaded, 16)
            sp.dma_start(w2_sb[:, :, :], w2.rearrange("(g p) n -> p g n", p=P)).then_inc(head_loaded, 16)
            sp.dma_start(w3_sb[:, :], w3).then_inc(head_loaded, 16)
            sp.dma_start(b1_sb[:, :], b1).then_inc(head_loaded, 16)
            sp.dma_start(b2_sb[:, :], b2).then_inc(head_loaded, 16)
            for x in range(NPASS):
                for n in SPLIT_AT[x]:
                    if n >= DIRECT:
                        move_lo(n)
                if x == QUADS + 1:
                    place_dense(0)
                for n, (first, _) in enumerate(LOADS):
                    if n >= K_RING and first - LOAD_AHEAD == x:
                        load_weights(n)
            place_dense(HALVES - 1)
            sp.wait_ge(head_kept, HALVES * len(PIECES))
            sp.dma_start(y.rearrange("(p t) o -> p (t o)", p=P), y_sb[:, :]).then_inc(y_stored, 16)
            sp.wait_ge(y_stored, 16)

        @block.gpsimd
        def _(pool):
            def gather_couple(n):
                h, m = divmod(n, COUPLES)
                if n >= G_RING:
                    pool.wait_ge(couple_transposed, n - G_RING + 1)
                for s in range(2):
                    for t in range(SUBS):
                        f = 2 * m + s
                        pool.indirect_dma_start(
                            gathered[:, n % G_RING, t, s * EMBED:(s + 1) * EMBED], None, tables[f],
                            bass.IndirectOffsetOnAxis(ap=ids_sb[:, h * SUBS + t, f:f + 1], axis=0),
                        ).then_inc(couple_gathered[n % G_RING], 16)

            def split_lo(s):
                load, at = LOAD_OF[s]
                pool.wait_ge(k_hi_ready, s + 1)
                pool.tensor_tensor(k_lo[:, s % S_RING, :], k_raw[:, load % K_RING, at, :],
                                   k_hi[:, s % S_RING, :].bitcast(F32), ALU.subtract).then_inc(k_lo_by_pool, 1)

            pool.wait_ge(ids_loaded, 16)
            for x in range(NPASS):
                for n in GATHERED_AT[x]:
                    gather_couple(n)
                for s in prepared_at(x, LO_AHEAD):
                    if lo_by_pool(s):
                        split_lo(s)

        @block.scalar
        def _(act):
            def split_hi(s):
                load, at = LOAD_OF[s]
                act.wait_ge(k_loaded[load % K_RING], 32 * (load // K_RING + 1))
                if s >= S_RING:
                    act.wait_ge(block_done, QUAD * (s - S_RING + 1))
                act.activation(k_hi[:, s % S_RING, :], k_raw[:, load % K_RING, at, :], ACT.Copy)\
                   .then_inc(k_hi_ready, 1)

            def keep_couple(n):
                act.wait_ge(couple_transposed, n + 1)
                act.activation(emb[:, n // COUPLES, n % COUPLES, :], side_ps[:, :], ACT.Copy).then_inc(emb_kept, 1)

            def split_couple_hi(n):
                h, m = divmod(n, COUPLES)
                act.wait_ge(emb_kept, n + 1)
                if n >= DIRECT:
                    act.wait_ge(emb_lo, n - 1)
                    act.activation(couple_hi[:, n % 2, :], emb[:, h, m, :], ACT.Copy).then_inc(couple_hi_ready, 1)
                if n >= E_RING:
                    ph, pm = divmod(n - E_RING, COUPLES)
                    act.wait_ge(block_done, ph * NBLK + NEEDED_TO[pm])
                act.activation(split[0:EMBED, n % E_RING, 0, :], emb[0:EMBED, h, m, :], ACT.Copy)
                act.activation(split[EMBED:P, n % E_RING, 1, :], emb[EMBED:P, h, m, :], ACT.Copy).then_inc(emb_hi, 1)

            def mix(h, m):
                if mixed_done(h, m):
                    act.wait_ge(duo_multiplied, (mixed_done(h, m) + 1) // 2)
                act.wait_ge(emb_kept, h * COUPLES + m + 1)
                for i in range(MIXED):
                    act.activation(emb[0:EMBED, h, COUPLES + i, :], emb[i * EMBED:(i + 1) * EMBED, h, m, :], ACT.Copy)
                for i in range(MIXED):
                    last = act.activation(emb[EMBED:P, h, COUPLES + i, :], emb[EMBED:P, h, m - 1, :], ACT.Copy)
                last.then_inc(mixed_kept, 1)

            def copy_z(i):
                last, h, g = FILLED[i]
                act.wait_ge(pass_reduced, last + 1)
                if h:
                    act.wait_ge(head_done, (h - 1) * len(PIECES) + MT1)
                act.activation(z_sb[:, g, :], z_ps[:, :], ACT.Copy).then_inc(z_copied, 1)

            def keep_head(h, i, bank):
                act.wait_ge(head_done, h * len(PIECES) + i + 1)
                layer, n = PIECES[i]
                if layer == "l1":
                    out = act.activation(h1_sb[:, n, :], bank, ACT.Relu, bias=b1_sb[:, n:n + 1])
                elif layer == "l2":
                    out = act.activation(h2_sb[:, n, :], bank, ACT.Relu, bias=b2_sb[:, n:n + 1])
                else:
                    out = act.activation(y_sb[:, h * SUBS:(h + 1) * SUBS], bank[:, 0:SUBS], ACT.Copy)
                out.then_inc(head_kept, 1)

            for x in range(NPASS):
                if x == 0:
                    for s in prepared_at(x, HI_AHEAD):
                        split_hi(s)
                for n in sorted({*TRANSPOSED_AT[x], *SPLIT_AT[x]}):
                    if n in TRANSPOSED_AT[x]:
                        keep_couple(n)
                    if n in SPLIT_AT[x]:
                        split_couple_hi(n)
                for h, m in MIXES:
                    if mix_pass(h, m) == x:
                        mix(h, m)
                if x > 0:
                    for s in prepared_at(x, HI_AHEAD):
                        split_hi(s)
                for i, (last, _, _) in enumerate(FILLED):
                    if last + 1 == x:
                        copy_z(i)
                if x == QUADS:
                    act.wait_ge(head_loaded, 16 * 5)
                if x in HEAD_AT:
                    keep_head(0, HEAD_AT[x], side_ps[:, :])
            copy_z(len(FILLED) - 1)
            for i in range(len(PIECES)):
                keep_head(HALVES - 1, i, bil_banks[i % len(bil_banks)])

        @block.vector
        def _(dve):
            def split_lo(s):
                load, at = LOAD_OF[s]
                dve.wait_ge(k_hi_ready, s + 1)
                dve.tensor_tensor(k_lo[:, s % S_RING, :], k_raw[:, load % K_RING, at, :],
                                  k_hi[:, s % S_RING, :].bitcast(F32), ALU.subtract).then_inc(k_lo_by_dve, 1)

            def split_couple(n):
                h, m = divmod(n, COUPLES)
                dve.wait_ge(emb_hi, n + 1)
                dve.tensor_tensor(split[EMBED:P, n % E_RING, 0, :], emb[0:EMBED, h, m, :],
                                  split[0:EMBED, n % E_RING, 0, :].bitcast(F32), ALU.subtract)
                dve.tensor_tensor(split[0:EMBED, n % E_RING, 1, :], emb[EMBED:P, h, m, :],
                                  split[EMBED:P, n % E_RING, 1, :].bitcast(F32), ALU.subtract).then_inc(emb_lo, 1)

            def split_couple_for_dma(n):
                h, m = divmod(n, COUPLES)
                dve.wait_ge(couple_hi_ready, n - DIRECT + 1)
                if moved_count(n - 2):
                    dve.wait_ge(emb_moved[(n - 2) % E_RING], 32 * moved_count(n - 2))
                dve.tensor_tensor(couple_lo[:, n % 2, :], emb[:, h, m, :],
                                  couple_hi[:, n % 2, :].bitcast(F32), ALU.subtract).then_inc(emb_lo, 1)

            def multiply(d):
                h, b = divmod(2 * d, NBLK)
                (_, _, _, ta, _), (_, _, _, tb, last_couple) = BLOCKS[b:b + 2]
                dve.wait_ge(block_done, 2 * d + 2)
                if d >= Y_RING:
                    dve.wait_ge(pass_reduced, (d - Y_RING) // 2 + 1)
                dve.wait_ge(emb_kept, h * COUPLES + last_couple + 1)
                if max(ta, tb) >= COUPLES:
                    mixed = [block[4] for block in BLOCKS[b:b + 2] if block[3] >= COUPLES][-1]
                    dve.wait_ge(mixed_kept, (h * COUPLES + mixed + 1) // 2)
                out, duo = prod[:, d % Y_RING, :, :], bil[d % B_RING]
                if tb > ta:
                    dve.tensor_tensor(out, duo[:, :, :], emb[:, h, ta:tb + 1:tb - ta, :], ALU.mult)\
                       .then_inc(duo_multiplied, 1)
                else:
                    dve.tensor_tensor(out[:, 0, :], duo[:, 0, :], emb[:, h, ta, :], ALU.mult)
                    dve.tensor_tensor(out[:, 1, :], duo[:, 1, :], emb[:, h, tb, :], ALU.mult)\
                       .then_inc(duo_multiplied, 1)

            for x in range(NPASS):
                for s in prepared_at(x, LO_AHEAD):
                    if x == 0 and not lo_by_pool(s):
                        split_lo(s)
                for n in SPLIT_AT[x]:
                    if n < DIRECT:
                        split_couple(n)
                multiply(2 * x)
                for s in prepared_at(x, LO_AHEAD):
                    if x > 0 and not lo_by_pool(s):
                        split_lo(s)
                multiply(2 * x + 1)
                for n in SPLIT_AT[x]:
                    if n >= DIRECT:
                        split_couple_for_dma(n)

        @block.tensor
        def _(pe):
            def transpose_couple(x, n):
                pe.wait_ge(couple_gathered[n % G_RING], 16 * 2 * SUBS * (n // G_RING + 1))
                if n:
                    pe.wait_ge(emb_kept, n)
                tiles = sum(at < x for at in HEAD_AT)
                if tiles:
                    pe.wait_ge(head_kept, tiles)
                for t in range(SUBS):
                    last = pe.transpose(side_ps[:, t * P:(t + 1) * P], gathered[:, n % G_RING, t, :], ident_sb[:, :])
                last.then_inc(couple_transposed, 1)

            def wait_moving(n):
                if n < DIRECT:
                    pe.wait_ge(emb_lo, n + 1)
                else:
                    pe.wait_ge(emb_hi, n + 1)
                    pe.wait_ge(emb_moved[n % E_RING], 32 * moved_count(n))

            def bilinear(x, c):
                b = QUAD * x + c
                h, hb = divmod(b, NBLK)
                j = BLOCKS[hb][0]
                n = h * COUPLES + j // 2
                if c == 0:
                    if lo_by_pool(x):
                        pe.wait_ge(k_lo_by_pool, lo_count(x, True))
                    else:
                        pe.wait_ge(k_lo_by_dve, lo_count(x, False))
                if hb == 0 or BLOCKS[hb - 1][0] // 2 != j // 2:
                    wait_moving(n)
                if b % 2 == 0 and b >= 2 * B_RING:
                    pe.wait_ge(duo_multiplied, b // 2 - B_RING + 1)
                out, moving = bil[b // 2 % B_RING][:, b % 2, :], split[:, n % E_RING, j % 2, :]
                cols = slice(c * P, (c + 1) * P)
                pe.matmul(out, k_hi[:, x % S_RING, cols], moving, start=True, stop=False)
                pe.matmul(out, k_lo[:, x % S_RING, cols], moving, start=False, stop=True).then_inc(block_done, 1)

            def reduce_pass(x):
                h, q = divmod(x, QUADS)
                group, k = divmod(q, GROUP_QUADS)
                pe.wait_ge(duo_multiplied, 2 * x + 2)
                if k == 0 and x:
                    pe.wait_ge(z_copied, h * GROUPS + group)
                for c in range(QUAD):
                    last = pe.matmul(z_ps[32 * c:32 * (c + 1), :], sel_sb[:, SEL_WIDTH - 32 - 2 * k:SEL_WIDTH - 2 * k],
                                     prod[:, (2 * x + c // 2) % Y_RING, c % 2, :],
                                     start=k == 0, stop=k == GROUP_QUADS - 1 or q == QUADS - 1,
                                     tile_position=(0, 32 * c))
                last.then_inc(pass_reduced, 1)

            def head(h, i, bank):
                layer, n = PIECES[i]
                pe.wait_ge(head_kept, h * len(PIECES) + i)
                if layer == "l1":
                    pe.wait_ge(dense_placed, 16 * len(FREE_ROWS) * (h + 1))
                    for g in range(GROUPS):
                        last = pe.matmul(bank, w1_sb[:, g, n * P:(n + 1) * P], z_sb[:, g, :],
                                         start=g == 0, stop=g == GROUPS - 1)
                elif layer == "l2":
                    for g in range(MT1):
                        last = pe.matmul(bank, w2_sb[:, g, n * P:(n + 1) * P], h1_sb[:, g, :],
                                         start=g == 0, stop=g == MT1 - 1)
                else:
                    outputs(bank)
                    return
                last.then_inc(head_done, 1)

            def outputs(bank):
                for t in range(SUBS):
                    for g in range(MT2):
                        last = pe.matmul(bank[:, t:t + 1], h2_sb[:, g, t * P:(t + 1) * P], w3_sb[:, g:g + 1],
                                         start=g == 0, stop=g == MT2 - 1)
                last.then_inc(head_done, 1)

            pe.wait_ge(consts_loaded, 32)
            for x in range(NPASS):
                for n in TRANSPOSED_AT[x]:
                    transpose_couple(x, n)
                for c in range(QUAD):
                    bilinear(x, c)
                if x and x % REDUCED == 0:
                    for multiplied in range(x - REDUCED, x):
                        reduce_pass(multiplied)
                if x == QUADS:
                    pe.wait_ge(head_loaded, 16 * 5)
                if x in HEAD_AT:
                    pe.wait_ge(emb_kept, sum(len(couples) for couples in TRANSPOSED_AT[:x + 1]))
                    head(0, HEAD_AT[x], side_ps[:, :])
            for multiplied in range(NPASS - REDUCED, NPASS):
                reduce_pass(multiplied)

            pe.wait_ge(duo_multiplied, 2 * NPASS)
            done = (HALVES - 1) * len(PIECES)
            for g in range(GROUPS):
                pe.wait_ge(z_copied, (HALVES - 1) * GROUPS + g + 1)
                if g == GROUPS - 1:
                    pe.wait_ge(dense_placed, 16 * len(FREE_ROWS) * HALVES)
                for n in range(MT1):
                    last = pe.matmul(bil_banks[n], w1_sb[:, g, n * P:(n + 1) * P], z_sb[:, g, :],
                                     start=g == 0, stop=g == GROUPS - 1)
                    if g == GROUPS - 1:
                        last.then_inc(head_done, 1)
            for n in range(MT2):
                for g in range(MT1):
                    pe.wait_ge(head_kept, done + g + 1)
                    last = pe.matmul(bil_banks[MT1 + n], w2_sb[:, g, n * P:(n + 1) * P], h1_sb[:, g, :],
                                     start=g == 0, stop=g == MT1 - 1)
                last.then_inc(head_done, 1)
            pe.wait_ge(head_kept, done + MT1 + MT2)
            outputs(bil_banks[0])



def kernel(**inputs):
    import concourse.bacc as bacc
    from concourse.bass_utils import run_bass_kernel_spmd

    get = {k: np.asarray(v) for k, v in inputs.items()}

    k = get["L0_rec_kernel"]
    k_blocks = np.empty((EMBED, NBLK, 2, EMBED), k.dtype)
    order = np.full((GROUPS, P), -1, np.int64)
    for b, (j, above, below, _, _) in enumerate(BLOCKS):
        for s, i in enumerate((above, below)):
            pair = pair_index(min(i, j), max(i, j))
            k_blocks[:, b, s] = k[:, pair] if i < j else k[:, pair].T
            order[z_row(b, s)] = pair
    order[order < 0] = FIELDS * (FIELDS - 1) // 2 + np.arange(DENSE)

    selector = np.zeros((P, SEL_WIDTH), np.float32)
    for s in range(2):
        selector[s * EMBED:(s + 1) * EMBED, SEL_WIDTH - 32 + s] = 1.0

    dense = get["dense_ctx"].reshape(P, TILES, DENSE).transpose(2, 1, 0).reshape(DENSE, BATCH)
    arrays = {
        "ids": get["ids"],
        "dense_rows": dense,
        "k_blocks": k_blocks.reshape(EMBED, -1),
        "w1": get["W_top1"][order.ravel()],
        "b1": get["b_top1"].reshape(MT1, P).T,
        "w2": get["W_top2"],
        "b2": get["b_top2"].reshape(MT2, P).T,
        "w3": get["W_top3"].reshape(MT2, P).T,
        "ident": np.eye(P, dtype=np.float32),
        "selector": selector,
    }
    arrays |= {f"tbl_{f}": get[f"tbl_{f}"] for f in range(FIELDS)}
    arrays = {f"in_{name}": np.ascontiguousarray(a) for name, a in arrays.items()}

    nc = bacc.Bacc("TRN2", target_bir_lowering=False, num_devices=1)
    aps = {name[3:]: nc.dram_tensor(name, a.shape, mybir.dt.from_np(a.dtype), kind="ExternalInput").ap()
           for name, a in arrays.items()}
    y = nc.dram_tensor("out_y", (BATCH, 1), F32, kind="ExternalOutput").ap()
    tables = [aps.pop(f"tbl_{f}") for f in range(FIELDS)]
    interaction_tower(nc, tables=tables, y=y, **aps)
    r = run_bass_kernel_spmd(nc, [arrays], core_ids=[0])
    return r.results[0]["out_y"]
```
